# Optimizing a Trainium2 kernel written in Bass

```python
import numpy as np
import jax
import jax.numpy as jnp

def _softmax(x, axis=-1):
    return jax.nn.softmax(x, axis=axis)

def _gelu(x):
    return jax.nn.gelu(x, approximate=True)

def _silu(x):
    return jax.nn.silu(x)

def _sigmoid(x):
    return jax.nn.sigmoid(x)

def _layernorm(x, axis=-1, eps=1e-05):
    m = jnp.mean(x, axis=axis, keepdims=True)
    v = jnp.var(x, axis=axis, keepdims=True)
    return (x - m) / jnp.sqrt(v + eps)

def _scatter_add(tgt, idx, src, axis=0):
    return tgt.at[idx].add(src)

def _segment_sum(src, seg, n):
    return jax.ops.segment_sum(src, seg, n)
kernel_name = 'mk_dlrm_tower_d1_rec_r8_011a5e'

def setup_inputs(seed: int=0):
    np.random.seed(seed)
    _w = jnp.asarray

    def _rec_inputs():
        import jax
        import jax.numpy as jnp
        _tk = jax.random.key(seed)
        ids = jnp.stack([jax.random.randint(jax.random.fold_in(_tk, 200 + f), (2048,), 0, v, jnp.int32) for f, v in enumerate([1000, 1250, 12500, 1250, 125000, 1250, 12500, 1000, 1000, 1250, 1000, 12500, 1250, 12500, 1000, 1250, 12500, 1000, 1000, 1000, 12500, 1250, 1000, 1000, 1250, 1000])], axis=1)
        tbl_0 = 0.05 * jax.random.normal(jax.random.fold_in(_tk, 500 + 0), (1000, 128), jnp.float32)
        tbl_1 = 0.05 * jax.random.normal(jax.random.fold_in(_tk, 500 + 1), (1250, 128), jnp.float32)
        tbl_2 = 0.05 * jax.random.normal(jax.random.fold_in(_tk, 500 + 2), (12500, 128), jnp.float32)
        tbl_3 = 0.05 * jax.random.normal(jax.random.fold_in(_tk, 500 + 3), (1250, 128), jnp.float32)
        tbl_4 = 0.05 * jax.random.normal(jax.random.fold_in(_tk, 500 + 4), (125000, 128), jnp.float32)
        tbl_5 = 0.05 * jax.random.normal(jax.random.fold_in(_tk, 500 + 5), (1250, 128), jnp.float32)
        tbl_6 = 0.05 * jax.random.normal(jax.random.fold_in(_tk, 500 + 6), (12500, 128), jnp.float32)
        tbl_7 = 0.05 * jax.random.normal(jax.random.fold_in(_tk, 500 + 7), (1000, 128), jnp.float32)
        tbl_8 = 0.05 * jax.random.normal(jax.random.fold_in(_tk, 500 + 8), (1000, 128), jnp.float32)
        tbl_9 = 0.05 * jax.random.normal(jax.random.fold_in(_tk, 500 + 9), (1250, 128), jnp.float32)
        tbl_10 = 0.05 * jax.random.normal(jax.random.fold_in(_tk, 500 + 10), (1000, 128), jnp.float32)
        tbl_11 = 0.05 * jax.random.normal(jax.random.fold_in(_tk, 500 + 11), (12500, 128), jnp.float32)
        tbl_12 = 0.05 * jax.random.normal(jax.random.fold_in(_tk, 500 + 12), (1250, 128), jnp.float32)
        tbl_13 = 0.05 * jax.random.normal(jax.random.fold_in(_tk, 500 + 13), (12500, 128), jnp.float32)
        tbl_14 = 0.05 * jax.random.normal(jax.random.fold_in(_tk, 500 + 14), (1000, 128), jnp.float32)
        tbl_15 = 0.05 * jax.random.normal(jax.random.fold_in(_tk, 500 + 15), (1250, 128), jnp.float32)
        tbl_16 = 0.05 * jax.random.normal(jax.random.fold_in(_tk, 500 + 16), (12500, 128), jnp.float32)
        tbl_17 = 0.05 * jax.random.normal(jax.random.fold_in(_tk, 500 + 17), (1000, 128), jnp.float32)
        tbl_18 = 0.05 * jax.random.normal(jax.random.fold_in(_tk, 500 + 18), (1000, 128), jnp.float32)
        tbl_19 = 0.05 * jax.random.normal(jax.random.fold_in(_tk, 500 + 19), (1000, 128), jnp.float32)
        tbl_20 = 0.05 * jax.random.normal(jax.random.fold_in(_tk, 500 + 20), (12500, 128), jnp.float32)
        tbl_21 = 0.05 * jax.random.normal(jax.random.fold_in(_tk, 500 + 21), (1250, 128), jnp.float32)
        tbl_22 = 0.05 * jax.random.normal(jax.random.fold_in(_tk, 500 + 22), (1000, 128), jnp.float32)
        tbl_23 = 0.05 * jax.random.normal(jax.random.fold_in(_tk, 500 + 23), (1000, 128), jnp.float32)
        tbl_24 = 0.05 * jax.random.normal(jax.random.fold_in(_tk, 500 + 24), (1250, 128), jnp.float32)
        tbl_25 = 0.05 * jax.random.normal(jax.random.fold_in(_tk, 500 + 25), (1000, 128), jnp.float32)
        _rk = jax.random.fold_in(_tk, 7)
        r_dense_output = -0.000520686 + 1.00062 * jax.random.normal(jax.random.fold_in(_rk, 101), (2048, 128), jnp.float32)
        W_top1 = 0.0405887 * jax.random.normal(jax.random.fold_in(_tk, 801), (607, 512), jnp.float32)
        W_top2 = 0.0441942 * jax.random.normal(jax.random.fold_in(_tk, 802), (512, 256), jnp.float32)
        W_top3 = 0.0625 * jax.random.normal(jax.random.fold_in(_tk, 803), (256, 1), jnp.float32)
        b_top1 = jnp.zeros((512,), jnp.float32)
        b_top2 = jnp.zeros((256,), jnp.float32)
        return (r_dense_output, ids, tbl_0, tbl_1, tbl_2, tbl_3, tbl_4, tbl_5, tbl_6, tbl_7, tbl_8, tbl_9, tbl_10, tbl_11, tbl_12, tbl_13, tbl_14, tbl_15, tbl_16, tbl_17, tbl_18, tbl_19, tbl_20, tbl_21, tbl_22, tbl_23, tbl_24, tbl_25, W_top1, b_top1, W_top2, b_top2, W_top3)
    r_dense_output, ids, tbl_0, tbl_1, tbl_2, tbl_3, tbl_4, tbl_5, tbl_6, tbl_7, tbl_8, tbl_9, tbl_10, tbl_11, tbl_12, tbl_13, tbl_14, tbl_15, tbl_16, tbl_17, tbl_18, tbl_19, tbl_20, tbl_21, tbl_22, tbl_23, tbl_24, tbl_25, W_top1, b_top1, W_top2, b_top2, W_top3 = _rec_inputs()

    def _L0_rec_setup():
        import jax, jax.numpy as jnp
        import numpy as np
        B, NUM_SPARSE, D = (2048, 26, 128)
        key = jax.random.key(seed)
        k1, k2 = jax.random.split(key)
        dense_output = jax.random.normal(k1, (B, D), dtype=jnp.float32)
        embeddings = jax.random.normal(k2, (B, NUM_SPARSE, D), dtype=jnp.float32)
        return {'dense_output': dense_output, 'embeddings': embeddings}
    _L0_rec_all = _L0_rec_setup()
    _L0_rec_in = {k: v for k, v in _L0_rec_all.items() if k in ()}
    del _L0_rec_all
    return {'r_dense_output': r_dense_output, 'ids': ids, 'tbl_0': tbl_0, 'tbl_1': tbl_1, 'tbl_2': tbl_2, 'tbl_3': tbl_3, 'tbl_4': tbl_4, 'tbl_5': tbl_5, 'tbl_6': tbl_6, 'tbl_7': tbl_7, 'tbl_8': tbl_8, 'tbl_9': tbl_9, 'tbl_10': tbl_10, 'tbl_11': tbl_11, 'tbl_12': tbl_12, 'tbl_13': tbl_13, 'tbl_14': tbl_14, 'tbl_15': tbl_15, 'tbl_16': tbl_16, 'tbl_17': tbl_17, 'tbl_18': tbl_18, 'tbl_19': tbl_19, 'tbl_20': tbl_20, 'tbl_21': tbl_21, 'tbl_22': tbl_22, 'tbl_23': tbl_23, 'tbl_24': tbl_24, 'tbl_25': tbl_25, 'W_top1': W_top1, 'b_top1': b_top1, 'W_top2': W_top2, 'b_top2': b_top2, 'W_top3': W_top3}

def reference(r_dense_output, ids, tbl_0, tbl_1, tbl_2, tbl_3, tbl_4, tbl_5, tbl_6, tbl_7, tbl_8, tbl_9, tbl_10, tbl_11, tbl_12, tbl_13, tbl_14, tbl_15, tbl_16, tbl_17, tbl_18, tbl_19, tbl_20, tbl_21, tbl_22, tbl_23, tbl_24, tbl_25, W_top1, b_top1, W_top2, b_top2, W_top3):
    import jax
    import jax.numpy as jnp

    def _L0_rec_ref(dense_output, embeddings):
        import jax, jax.numpy as jnp
        import numpy as np
        B, NUM_SPARSE, D = (2048, 26, 128)
        combined = jnp.concatenate([dense_output[:, None, :], embeddings], axis=1)
        interactions = jnp.einsum('bfd,bgd->bfg', combined, combined)
        F = combined.shape[1]
        iu, ju = jnp.triu_indices(F, k=1)
        interactions_flat = interactions[:, iu, ju]
        return jnp.concatenate([dense_output, interactions_flat], axis=1)
    e = jnp.stack([tbl_0[ids[:, 0]], tbl_1[ids[:, 1]], tbl_2[ids[:, 2]], tbl_3[ids[:, 3]], tbl_4[ids[:, 4]], tbl_5[ids[:, 5]], tbl_6[ids[:, 6]], tbl_7[ids[:, 7]], tbl_8[ids[:, 8]], tbl_9[ids[:, 9]], tbl_10[ids[:, 10]], tbl_11[ids[:, 11]], tbl_12[ids[:, 12]], tbl_13[ids[:, 13]], tbl_14[ids[:, 14]], tbl_15[ids[:, 15]], tbl_16[ids[:, 16]], tbl_17[ids[:, 17]], tbl_18[ids[:, 18]], tbl_19[ids[:, 19]], tbl_20[ids[:, 20]], tbl_21[ids[:, 21]], tbl_22[ids[:, 22]], tbl_23[ids[:, 23]], tbl_24[ids[:, 24]], tbl_25[ids[:, 25]]], axis=1)
    z = _L0_rec_ref(r_dense_output, e)
    z = z.reshape(z.shape[0], -1)
    h = jnp.concatenate([z, r_dense_output], axis=1)
    h = jnp.maximum(h @ W_top1 + b_top1, 0.0)
    h = jnp.maximum(h @ W_top2 + b_top2, 0.0)
    y = h @ W_top3
    return y

_drawn_inputs = setup_inputs


def setup_inputs(seed=0):
    import zlib

    import numpy as np

    out = dict(_drawn_inputs(seed))
    spreads = {'b_top1': (0.0, 0.1), 'b_top2': (0.0, 0.1)}
    factors = {}
    for name, (base, spread) in spreads.items():
        noise = np.random.default_rng([zlib.crc32(name.encode()), seed]).standard_normal(out[name].shape)
        drawn = base * np.exp(spread * noise) if base else spread * noise
        out[name] = jnp.asarray(drawn.astype(out[name].dtype))
    for name, factor in factors.items():
        out[name] = (out[name] * factor).astype(out[name].dtype)
    return out
```

```python
from contextlib import ExitStack

import concourse.bass as bass
from concourse import mybir

F32 = mybir.dt.float32
BF16 = mybir.dt.bfloat16
I16 = mybir.dt.int16
I32 = mybir.dt.int32
ALU = mybir.AluOpType
ACT = mybir.ActivationFunctionType

P = 128
D = 128
TABLE_ROWS = [1000, 1250, 12500, 1250, 125000, 1250, 12500, 1000, 1000, 1250, 1000, 12500, 1250,
              12500, 1000, 1250, 12500, 1000, 1000, 1000, 12500, 1250, 1000, 1000, 1250, 1000]
SELECTED = [0, 7, 8, 10, 14]
FETCHED = [f for f in range(len(TABLE_ROWS)) if f not in SELECTED]
SLOTS = [0] + [1 + f for f in SELECTED] + [1 + f for f in FETCHED]
F = len(SLOTS)
K_MAX = (F - 1) // 2
PAIRS = F * (F - 1) // 2
ZC = 3
ZK = PAIRS // ZC
SUB = 32
QUADS = P // SUB
ROWS = 1000
CHUNKS = 8
CR = ROWS // CHUNKS
PARTS = 3
NS = len(SELECTED)
NF = len(FETCHED)
S0 = 1 + NS
GROUP = 4
GROUPS = [(s, min(s + GROUP, F)) for s in range(S0, F, GROUP)]
NG = len(GROUPS)
TURNS = NG + 1
GRAMS = 4
GB = SUB // GRAMS


def pair_rows():
    first = {}
    n = D
    for a in range(F):
        for b in range(a + 1, F):
            first[a, b] = n
            n += 1
    rows = []
    for k in range(1, K_MAX + 1):
        for f in range(F):
            a, b = SLOTS[f], SLOTS[(f + k) % F]
            rows.append(first[min(a, b), max(a, b)])
    return rows


def tower(nc, dense_t, ids_fetched, ids_selected, tables, w1_pairs, w1_dense, w2, w3, b1, b2, out):
    B = dense_t.shape[1]
    H1 = w1_dense.shape[2]
    H2 = w2.shape[1]
    C1, C2 = H1 // P, H2 // P
    N = 2 * P
    NP = B // N
    MLPS = C1 + C2 + 1
    assert C1 == GRAMS and MLPS == 2 * GRAMS - 1 and NS <= GRAMS + 1

    with ExitStack() as ctx:
        def sb(name, shape, dt):
            return ctx.enter_context(nc.sbuf_tensor(name, shape, dt))

        def psum(name, shape):
            return ctx.enter_context(nc.psum_tensor(name, shape, F32))

        def sem(name):
            return ctx.enter_context(nc.semaphore(name))

        ident = sb("ident", [P, P], F32)
        row_i = sb("row_i", [CR, CHUNKS], I32)
        row_id = sb("row_id", [CR, CHUNKS], F32)
        w1z = sb("w1z", [ZK, ZC, H1], F32)
        w1ab = sb("w1ab", [P, 2, H1], F32)
        w1d = sb("w1d", [P, H1], F32)
        w2s = sb("w2s", [P, C1, H2], F32)
        w3s = sb("w3s", [P, C2], F32)
        b1s = sb("b1s", [P, C1], F32)
        b2s = sb("b2s", [P, C2], F32)
        rest = sb("rest", [CR, NS, CHUNKS * D], F32)
        parts = sb("parts", [CR, NS, PARTS, CHUNKS * D], BF16)
        idx = sb("idx", [P, 2, NF], I32)
        rows = sb("rows", [P, 2, NF, D], F32)
        ids_b = sb("ids_b", [CR, NS, N], I32)
        ids_s = sb("ids_s", [CR, NS, N], I16)
        onehot = sb("onehot", [CR, NS, CHUNKS, N], BF16)
        staged = sb("staged", [P, S0, N], F32)
        feat = sb("feat", [P, 2, P, SUB], F32)
        gram = sb("gram", [P, 2, F, SUB], F32)
        z = sb("z", [P, 2, F + K_MAX, SUB], F32)
        pairs = sb("pairs", [P, 2, K_MAX, F], F32)
        zt = sb("zt", [P, ZC + 1, N], F32)
        h1 = sb("h1", [P, C1, N], F32)
        h2 = sb("h2", [P, C2, N], F32)
        y = sb("y", [1, B], F32)

        turn_ps = psum("turn_ps", [P, 2, 512])
        gram_ps = psum("gram_ps", [P, 2, GB * P])
        pick_ps = psum("pick_ps", [P, 512])[:, 0:N]
        mlp_ps = psum("mlp_ps", [P, 512])[:, 0:N]

        ids_in = [sem(f"ids_in{u}") for u in range(2)]
        rows_in = [[sem(f"rows_in{u}_{g}") for g in range(NG)] for u in range(2)]
        ids_b_in = sem("ids_b_in")
        staged_in = sem("staged_in")
        zt_in = sem("zt_in")
        table_in = [sem(f"table_in{o}") for o in range(NS)]
        w1z_in = sem("w1z_in")
        w1ab_in = sem("w1ab_in")
        mlp_in = sem("mlp_in")
        y_out = sem("y_out")
        pool_passed = sem("pool_passed")
        sp_passed = sem("sp_passed")
        ident_zero = sem("ident_zero")
        ident_done = sem("ident_done")
        row_i_done = sem("row_i_done")
        row_id_done = sem("row_id_done")
        feat_zero = sem("feat_zero")
        w1d_done = sem("w1d_done")
        act_part = sem("act_part")
        dve_rest = sem("dve_rest")
        turned = sem("turned")
        turn_taken = sem("turn_taken")
        staged_taken = sem("staged_taken")
        ids_s_done = sem("ids_s_done")
        onehot_done = sem("onehot_done")
        picked = sem("picked")
        pick_taken = sem("pick_taken")
        grammed = sem("grammed")
        gram_taken = sem("gram_taken")
        z_done = sem("z_done")
        pairs_done = sem("pairs_done")
        layer = sem("layer")
        layer_taken = sem("layer_taken")
        rows_free = TURNS * 2

        block = ctx.enter_context(nc.Block())

        @block.sync
        def _(sp):
            def load_ids(i, u):
                sp.dma_start(idx[:, u, :], ids_fetched[bass.ds(i * N + u * P, P), :])\
                    .then_inc(ids_in[u], 16)

            def load_ids_b(i):
                sp.dma_start(ids_b[:, :, :], ids_selected[:, bass.ds(i * N, N)]
                             .rearrange("(a t) n -> a t n", a=1).to_broadcast([CR, NS, N]))\
                    .then_inc(ids_b_in, 16)

            def load_dense(i):
                sp.dma_start(staged[:, 0, :], dense_t[:, bass.ds(i * N, N)]).then_inc(staged_in, 16)

            def load_zt(i):
                sp.dma_start(zt[:, ZC, :], dense_t[:, bass.ds(i * N, N)]).then_inc(zt_in, 16)

            for u in range(2):
                load_ids(0, u)
            for o in range(NS):
                sp.dma_start(rest[:, o, :], tables[SELECTED[o]].rearrange("(r c) d -> r (c d)", c=CHUNKS))\
                    .then_inc(table_in[o], 16)
            load_ids_b(0)
            load_dense(0)
            load_zt(0)
            sp.dma_start(w1z[:, :, :], w1_pairs.rearrange("(c k) n -> k c n", c=ZC)).then_inc(w1z_in, 16)
            sp.dma_start(w1ab[:, :, :], w1_dense.rearrange("a k n -> k a n")).then_inc(w1ab_in, 16)
            sp.dma_start(w2s[:, :, :], w2.rearrange("(c k) n -> k c n", c=C1)).then_inc(mlp_in, 16)
            sp.dma_start(w3s[:, :], w3).then_inc(mlp_in, 16)
            sp.dma_start(b1s[:, :], b1).then_inc(mlp_in, 16)
            sp.dma_start(b2s[:, :], b2).then_inc(mlp_in, 16)
            sp.wait_ge(ids_s_done, 1)
            load_ids_b(1)

            def refill(i):
                for u in range(2):
                    sp.wait_ge(rows_in[u][NG - 1], (i + 1) * (16 * (GROUPS[-1][1] - GROUPS[-1][0])))
                    sp.sem_inc(sp_passed, 1)
                    load_ids(i + 1, u)
                    if u == 0:
                        sp.wait_ge(staged_taken, 2 * i + 2)
                        sp.sem_inc(sp_passed, 1)
                        load_dense(i + 1)
                sp.wait_ge(layer, i * MLPS + C1)
                sp.sem_inc(sp_passed, 1)
                load_zt(i + 1)

            with sp.Fori(0, NP - 2) as i:
                refill(i)
                sp.wait_ge(ids_s_done, i + 2)
                sp.sem_inc(sp_passed, 1)
                load_ids_b(i + 2)
            refill(NP - 2)
            sp.wait_ge(layer_taken, NP * MLPS + 1)
            sp.dma_start(out.rearrange("b a -> a b"), y[:, :]).then_inc(y_out, 16)
            sp.wait_ge(y_out, 16)

        @block.gpsimd
        def _(pool):
            pool.memset(ident[:, :], 0.0).then_inc(ident_zero, 1)
            pool.wait_ge(ident_zero, 1)
            pool.affine_select(out=ident[:, :], in_=ident[:, :], compare_op=ALU.not_equal, fill=1.0,
                               base=0, pattern=[[-1, P]], channel_multiplier=1).then_inc(ident_done, 1)
            pool.iota(row_i[:, :], pattern=[[1, CHUNKS]], base=0, channel_multiplier=CHUNKS)\
                .then_inc(row_i_done, 1)
            with pool.Fori(0, NP) as i:
                for u in range(2):
                    pool.wait_ge(ids_in[u], i * 16 + 16)
                    pool.sem_inc(pool_passed, 1)
                    for g, (a, b) in enumerate(GROUPS):
                        pool.wait_ge(turned, i * (2 * TURNS) + (u * TURNS + g + 1))
                        pool.sem_inc(pool_passed, 1)
                        for s in range(a, b):
                            n = s - S0
                            pool.indirect_dma_start(
                                rows[:, u, n, :], None, tables[FETCHED[n]],
                                bass.IndirectOffsetOnAxis(ap=idx[:, u, n:n + 1], axis=0))\
                                .then_inc(rows_in[u][g], 16)

        @block.tensor
        def _(pe):
            def turn_rows(i, u):
                for g, (a, b) in enumerate(GROUPS):
                    n = u * TURNS + g
                    pe.wait_ge(rows_in[u][g], i * (16 * (b - a)) + 16 * (b - a))
                    pe.wait_ge(turn_taken, i * (2 * TURNS) + n + 1)
                    for s in range(a, b):
                        t = pe.transpose(turn_ps[:, n % 2, (s - a) * P:(s - a + 1) * P],
                                         rows[:, u, s - S0, :], ident[:, :])
                    t.then_inc(turned, 1)

            def gram_blocks(i, u, c):
                if c == 0:
                    pe.wait_ge(turn_taken, i * (2 * TURNS) + (u * TURNS + NG + 2))
                pe.wait_ge(gram_taken, i * (2 * GRAMS) + (u * GRAMS + c + 1))
                for k in range(GB):
                    j = c * GB + k
                    m = pe.matmul(gram_ps[:, c % 2, k * P:k * P + QUADS * F]
                                  .rearrange("p (s g) -> p s g", s=QUADS),
                                  feat[:, u, j * QUADS:(j + 1) * QUADS, :].rearrange("d s f -> d (s f)"),
                                  feat[:, u, j * QUADS:(j + 1) * QUADS, 0:F],
                                  start=True, stop=True)
                m.then_inc(grammed, 1)

            def turn_pairs(i, u):
                n = u * TURNS + NG
                pe.wait_ge(pairs_done, i * 2 + u + 1)
                pe.wait_ge(turn_taken, i * (2 * TURNS) + n + 1)
                flat = pairs[:, u, :, :].rearrange("p k f -> p (k f)")
                for c in range(ZC):
                    t = pe.transpose(turn_ps[0:ZK, n % 2, c * P:(c + 1) * P],
                                     flat[:, c * ZK:(c + 1) * ZK], ident[:, :])
                t.then_inc(turned, 1)

            def pick(i, o):
                pe.wait_ge(onehot_done, i * NS + (o + 1))
                pe.wait_ge(pick_taken, i * NS + (o + 1))
                for c in range(CHUNKS):
                    for q in range(PARTS):
                        m = pe.matmul(pick_ps, parts[:, o, q, c * D:(c + 1) * D],
                                      onehot[:, o, c, :], start=(c == 0 and q == 0),
                                      stop=(c == CHUNKS - 1 and q == PARTS - 1))
                m.then_inc(picked, 1)

            def mlp(i, n):
                pe.wait_ge(layer_taken, i * MLPS + (n + 1))
                if n == 0:
                    pe.wait_ge(turn_taken, i * (2 * TURNS) + (2 * TURNS + 2))
                    pe.wait_ge(zt_in, i * 16 + 16)
                if n < C1:
                    for c in range(ZC):
                        pe.matmul(mlp_ps, w1z[:, c, n * P:(n + 1) * P], zt[0:ZK, c, :],
                                  start=(c == 0), stop=False)
                    h = pe.matmul(mlp_ps, w1d[:, n * P:(n + 1) * P], zt[:, ZC, :],
                                  start=False, stop=True)
                elif n < C1 + C2:
                    m = n - C1
                    for c in range(C1):
                        h = pe.matmul(mlp_ps, w2s[:, c, m * P:(m + 1) * P], h1[:, c, :],
                                      start=(c == 0), stop=(c == C1 - 1))
                else:
                    for c in range(C2):
                        h = pe.matmul(mlp_ps[0:1, :], w3s[:, c:c + 1], h2[:, c, :],
                                      start=(c == 0), stop=(c == C2 - 1))
                h.then_inc(layer, 1)

            pe.sem_inc(turned, rows_free)
            pe.wait_ge(ident_done, 1)
            for o in range(NS):
                pe.wait_ge(act_part, (PARTS - 1) * NS + o + 1)
                pick(0, o)
            pe.wait_ge(w1z_in, 16)
            pe.wait_ge(w1d_done, 1)
            pe.wait_ge(mlp_in, 64)

            def pair(i, first=False, last=False):
                turn_rows(i, 0)
                for c in range(GRAMS):
                    gram_blocks(i, 0, c)
                    if not first:
                        mlp(i - 1, c)
                if not last:
                    pick(i + 1, 0)
                turn_pairs(i, 0)
                turn_rows(i, 1)
                for c in range(GRAMS):
                    gram_blocks(i, 1, c)
                    if not first and c > 0:
                        mlp(i - 1, GRAMS + c - 1)
                    if not last and c + 1 < NS:
                        pick(i + 1, c + 1)
                turn_pairs(i, 1)

            pair(0, first=True)
            with pe.Fori(1, NP - 1) as i:
                pair(i)
            pair(NP - 1, last=True)
            for n in range(MLPS):
                mlp(NP - 1, n)

        @block.vector
        def _(dve):
            def make_onehot(i, first=False):
                dve.wait_ge(ids_b_in, i * 16 + 16)
                dve.tensor_copy(ids_s[:, :, :], ids_b[:, :, :]).then_inc(ids_s_done, 1)
                dve.wait_ge(ids_s_done, i + 1)
                for o in range(NS):
                    if not first:
                        dve.wait_ge(picked, (i - 1) * NS + (o + 1))
                    for c in range(CHUNKS):
                        t = dve.tensor_scalar(onehot[:, o, c, :], ids_s[:, o, :], row_id[:, c:c + 1],
                                              None, ALU.is_equal)
                    t.then_inc(onehot_done, 1)

            def place_staged(i, u):
                dve.wait_ge(pick_taken, i * NS + (NS + 1))
                dve.wait_ge(staged_in, i * 16 + 16)
                dve.tensor_copy(feat[:, u, :, 0:S0].rearrange("d p s -> d s p"),
                                staged[:, :, u * P:(u + 1) * P]).then_inc(staged_taken, 1)

            def place_rows(i, u):
                for g, (a, b) in enumerate(GROUPS):
                    n = u * TURNS + g
                    dve.wait_ge(turned, i * (2 * TURNS) + (rows_free + n + 1))
                    dve.tensor_copy(feat[:, u, :, a:b].rearrange("d p s -> d s p"),
                                    turn_ps[:, n % 2, 0:(b - a) * P].rearrange("d (s p) -> d s p", p=P))\
                        .then_inc(turn_taken, 1)

            def make_z(i, u):
                dve.wait_ge(gram_taken, i * (2 * GRAMS) + ((u + 1) * GRAMS + 2))
                dve.transpose(z[:, u, 0:F, :], gram[:, u, :, :])
                dve.transpose(z[:, u, F:F + K_MAX, :], gram[:, u, 0:K_MAX, :]).then_inc(z_done, 1)
                dve.wait_ge(z_done, i * 2 + (u + 3))
                flat = z[:, u, :, :].rearrange("p g f -> p (g f)")
                diagonals = bass.AP(flat.tensor, flat.offset + SUB,
                                    [list(flat.ap[0]), [SUB, K_MAX], [SUB + 1, F]])
                dve.tensor_copy(pairs[:, u, :, :], diagonals).then_inc(pairs_done, 1)

            def place_pairs(i, u):
                n = u * TURNS + NG
                dve.wait_ge(turned, i * (2 * TURNS) + (rows_free + n + 1))
                dve.tensor_copy(zt[0:ZK, 0:ZC, u * P:(u + 1) * P].rearrange("k c (j s) -> k c s j", s=QUADS),
                                turn_ps[0:ZK, n % 2, 0:ZC * P].rearrange("k (c s j) -> k c s j", c=ZC, s=QUADS))\
                    .then_inc(turn_taken, 1)

            dve.sem_inc(turn_taken, 2)
            dve.sem_inc(z_done, 2)
            for u in range(2):
                dve.memset(feat[:, u, :, F:SUB], 0.0).then_inc(feat_zero, 1)
            dve.wait_ge(row_i_done, 1)
            dve.tensor_copy(row_id[:, :], row_i[:, :]).then_inc(row_id_done, 1)
            dve.wait_ge(row_id_done, 1)
            make_onehot(0, first=True)
            for q in range(PARTS - 1):
                for o in range(NS):
                    dve.wait_ge(act_part, q * NS + o + 1)
                    dve.tensor_tensor(rest[:, o, :], rest[:, o, :], parts[:, o, q, :], ALU.subtract)\
                        .then_inc(dve_rest, 1)
            dve.wait_ge(w1ab_in, 16)
            dve.tensor_tensor(w1d[:, :], w1ab[:, 0, :], w1ab[:, 1, :], ALU.add).then_inc(w1d_done, 1)

            def pair(i, last):
                for u in range(2):
                    place_staged(i, u)
                place_rows(i, 0)
                if not last:
                    make_onehot(i + 1)
                make_z(i, 0)
                place_pairs(i, 0)
                place_rows(i, 1)
                make_z(i, 1)
                place_pairs(i, 1)

            with dve.Fori(0, NP - 1) as i:
                pair(i, False)
            pair(NP - 1, True)

        @block.scalar
        def _(act):
            def keep_grams(i, u, c):
                if c == 0:
                    act.wait_ge(z_done, i * 2 + (u + 1))
                act.wait_ge(grammed, i * (2 * GRAMS) + (u * GRAMS + c + 1))
                blocks = gram_ps[:, c % 2, :].rearrange("p (j x) -> p j x", j=GB)
                for s in range(QUADS):
                    q = slice(s * SUB, (s + 1) * SUB)
                    t = act.activation(gram[q, u, :, c * GB:(c + 1) * GB].rearrange("p g j -> p j g"),
                                       blocks[q, :, s * F:(s + 1) * F], ACT.Copy)
                t.then_inc(gram_taken, 1)

            def keep_pick(i, o):
                act.wait_ge(picked, i * NS + (o + 1))
                act.activation(staged[:, 1 + o, :], pick_ps, ACT.Copy).then_inc(pick_taken, 1)

            def keep_mlp(i, n):
                act.wait_ge(layer, i * MLPS + (n + 1))
                if n < C1:
                    t = act.activation(h1[:, n, :], mlp_ps, ACT.Relu, bias=b1s[:, n:n + 1])
                elif n < C1 + C2:
                    m = n - C1
                    t = act.activation(h2[:, m, :], mlp_ps, ACT.Relu, bias=b2s[:, m:m + 1])
                else:
                    t = act.activation(y[:, bass.ds(i * N, N)], mlp_ps[0:1, :], ACT.Copy)
                t.then_inc(layer_taken, 1)

            act.sem_inc(gram_taken, 2)
            act.sem_inc(pick_taken, 1)
            act.sem_inc(layer_taken, 1)
            for q in range(PARTS):
                for o in range(NS):
                    if q == 0:
                        act.wait_ge(table_in[o], 16)
                    else:
                        act.wait_ge(dve_rest, (q - 1) * NS + o + 1)
                    act.activation(parts[:, o, q, :], rest[:, o, :], ACT.Copy).then_inc(act_part, 1)
            act.wait_ge(mlp_in, 64)
            for o in range(NS):
                keep_pick(0, o)

            def pair(i, first=False, last=False):
                for c in range(GRAMS):
                    keep_grams(i, 0, c)
                    if not first:
                        keep_mlp(i - 1, c)
                if not last:
                    act.wait_ge(staged_taken, i * 2 + 2)
                    keep_pick(i + 1, 0)
                for c in range(GRAMS):
                    keep_grams(i, 1, c)
                    if not first and c > 0:
                        keep_mlp(i - 1, GRAMS + c - 1)
                    if not last and c + 1 < NS:
                        keep_pick(i + 1, c + 1)

            pair(0, first=True)
            with act.Fori(1, NP - 1) as i:
                pair(i)
            pair(NP - 1, last=True)
            for n in range(MLPS):
                keep_mlp(NP - 1, n)


def kernel(**inputs):
    import numpy as np
    import concourse.bacc as bacc
    from concourse.bass_utils import run_bass_kernel_spmd as run

    a = {k: np.asarray(v) for k, v in inputs.items()}
    ids, w1 = a["ids"], a["W_top1"]
    arrays = {
        "dense_t": a["r_dense_output"].T,
        "ids_fetched": ids[:, FETCHED],
        "ids_selected": ids[:, SELECTED].T,
        "w1_pairs": w1[pair_rows()],
        "w1_dense": np.stack([w1[:D], w1[D + PAIRS:]]),
        "w2": a["W_top2"],
        "w3": a["W_top3"].reshape(-1, P).T,
        "b1": a["b_top1"].reshape(-1, P).T,
        "b2": a["b_top2"].reshape(-1, P).T,
    }
    arrays |= {f"tbl_{f}": a[f"tbl_{f}"] for f in range(len(TABLE_ROWS))}
    arrays = {k: np.ascontiguousarray(v) for k, v in arrays.items()}

    nc = bacc.Bacc("TRN2", target_bir_lowering=False, num_devices=1)
    ap = {k: nc.dram_tensor(k, v.shape, mybir.dt.from_np(v.dtype), kind="ExternalInput").ap()
          for k, v in arrays.items()}
    out = nc.dram_tensor("y_out_dram", (ids.shape[0], 1), F32, kind="ExternalOutput").ap()
    tower(nc, ap["dense_t"], ap["ids_fetched"], ap["ids_selected"],
          [ap[f"tbl_{f}"] for f in range(len(TABLE_ROWS))], ap["w1_pairs"], ap["w1_dense"],
          ap["w2"], ap["w3"], ap["b1"], ap["b2"], out)
    return run(nc, [arrays], core_ids=[0]).results[0]["y_out_dram"]
```

```python
from contextlib import ExitStack

import concourse.bass as bass
from concourse import mybir

F32 = mybir.dt.float32
BF16 = mybir.dt.bfloat16
F16 = mybir.dt.float16
I32 = mybir.dt.int32
ALU = mybir.AluOpType
ACT = mybir.ActivationFunctionType

P = 128
D = 128
TABLE_ROWS = [1000, 1250, 12500, 1250, 125000, 1250, 12500, 1000, 1000, 1250, 1000, 12500, 1250,
              12500, 1000, 1250, 12500, 1000, 1000, 1000, 12500, 1250, 1000, 1000, 1250, 1000]
SELECTED = [0, 7, 8, 10, 14]
FETCHED = [f for f in range(len(TABLE_ROWS)) if f not in SELECTED]
SLOTS = [0] + [1 + f for f in SELECTED] + [1 + f for f in FETCHED]
F = len(SLOTS)
K_MAX = (F - 1) // 2
PAIRS = F * (F - 1) // 2
ZC = 3
ZK = PAIRS // ZC
SUB = 32
QUADS = P // SUB
ROWS = 1000
CHUNKS = 8
CR = ROWS // CHUNKS
PARTS = 3
NS = len(SELECTED)
NF = len(FETCHED)
S0 = 1 + NS
GROUP = 4
GROUPS = [(s, min(s + GROUP, F)) for s in range(S0, F, GROUP)]
NG = len(GROUPS)
GRAMS = 4
GB = SUB // GRAMS
TURNS = NG + 1
SKIPPED = 2
BANKS = 2


def group_turn(i, u, g):
    if isinstance(i, int) and i == 0:
        return SKIPPED + u * NG + g
    return i * (2 * TURNS) + (u * TURNS + (g + 1 if g else 0))


def pairs_turn(i, u, last=False):
    return i * (2 * TURNS) + (2 * TURNS + u if last else (u + 2) * TURNS + 1)


def turn_bank(u, g, first):
    return group_turn(0, u, g) % BANKS if first else (u * TURNS + (g + 1 if g else 0)) % BANKS


def pairs_bank(u, last):
    return pairs_turn(0, u, last) % BANKS


def pair_rows():
    first = {}
    n = D
    for a in range(F):
        for b in range(a + 1, F):
            first[a, b] = n
            n += 1
    rows = []
    for k in range(1, K_MAX + 1):
        for f in range(F):
            a, b = SLOTS[f], SLOTS[(f + k) % F]
            rows.append(first[min(a, b), max(a, b)])
    return rows


def part_order():
    return [(q, k - q) for k in range(NS + PARTS - 1) for q in range(PARTS) if 0 <= k - q < NS]


def tower(nc, dense_t, ids_fetched, ids_selected, tables, w1_pairs, w1_dense, w2, w3, b1, b2, out):
    B = dense_t.shape[1]
    H1 = w1_dense.shape[2]
    H2 = w2.shape[1]
    C1, C2 = H1 // P, H2 // P
    N = 2 * P
    NP = B // N
    MLPS = C1 + C2 + 1
    assert (C1, C2, GRAMS) == (4, 2, 4) and NS <= GRAMS + 1 and NG > GRAMS

    with ExitStack() as ctx:
        def sb(name, shape, dt):
            return ctx.enter_context(nc.sbuf_tensor(name, shape, dt))

        def psum(name, shape):
            return ctx.enter_context(nc.psum_tensor(name, shape, F32))

        def sem(name):
            return ctx.enter_context(nc.semaphore(name))

        ident = sb("ident", [P, P], F32)
        row_i = sb("row_i", [CR, CHUNKS], I32)
        row_id = sb("row_id", [CR, CHUNKS], F32)
        w1z = sb("w1z", [ZK, ZC, H1], F32)
        w1ab = sb("w1ab", [P, 2, H1], F32)
        w1d = sb("w1d", [P, H1], F32)
        w2s = sb("w2s", [P, C1, H2], F32)
        w3s = sb("w3s", [P, C2], F32)
        b1s = sb("b1s", [P, C1], F32)
        b2s = sb("b2s", [P, C2], F32)
        rest = sb("rest", [CR, NS, CHUNKS * D], F32)
        parts = sb("parts", [CR, NS, PARTS, CHUNKS * D], BF16)
        idx = sb("idx", [P, 2, NF], I32)
        rows = sb("rows", [P, 2, NF, D], F32)
        ids_b = sb("ids_b", [CR, NS, N], I32)
        ids_s = sb("ids_s", [CR, NS, N], F16)
        onehot = sb("onehot", [CR, NS, CHUNKS, N], BF16)
        staged = sb("staged", [P, S0, N], F32)
        feat = sb("feat", [P, 2, P, SUB], F32)
        gram = sb("gram", [P, 2, F, SUB], F32)
        z = sb("z", [P, 2, F + K_MAX, SUB], F32)
        pairs = sb("pairs", [P, 2, K_MAX, F], F32)
        zt = sb("zt", [P, ZC + 1, N], F32)
        h1 = sb("h1", [P, C1, N], F32)
        h2 = sb("h2", [P, C2, N], F32)
        y = sb("y", [1, B], F32)

        turn_ps = psum("turn_ps", [P, 2, 512])
        gram_ps = psum("gram_ps", [P, 2, GB * P])
        pick_ps = psum("pick_ps", [P, 512])[:, 0:N]
        mlp_ps = psum("mlp_ps", [P, 512])[:, 0:N]

        ids_in = [sem(f"ids_in{u}") for u in range(2)]
        rows_in = [[sem(f"rows_in{u}_{g}") for g in range(NG)] for u in range(2)]
        ids_b_in = sem("ids_b_in")
        staged_in = sem("staged_in")
        zt_in = sem("zt_in")
        table_in = [sem(f"table_in{o}") for o in range(NS)]
        w1z_in = sem("w1z_in")
        w1ab_in = sem("w1ab_in")
        mlp_in = sem("mlp_in")
        y_out = sem("y_out")
        pool_passed = sem("pool_passed")
        sp_passed = sem("sp_passed")
        ident_zero = sem("ident_zero")
        ident_done = sem("ident_done")
        row_i_done = sem("row_i_done")
        row_id_done = sem("row_id_done")
        feat_zero = sem("feat_zero")
        w1d_done = sem("w1d_done")
        act_part = sem("act_part")
        dve_rest = sem("dve_rest")
        turned = sem("turned")
        turn_taken = sem("turn_taken")
        staged_taken = sem("staged_taken")
        ids_s_done = sem("ids_s_done")
        onehot_done = sem("onehot_done")
        picked = sem("picked")
        pick_taken = sem("pick_taken")
        grammed = sem("grammed")
        gram_taken = sem("gram_taken")
        z_done = sem("z_done")
        pairs_done = sem("pairs_done")
        layer = sem("layer")
        layer_taken = sem("layer_taken")
        rows_free = TURNS * 2

        def layer_number(i, n, half=None):
            return i * MLPS + (n + (MLPS if half == 1 else 0))

        def layer_bank(number, two):
            return pick_ps if two and number % 2 else mlp_ps

        def columns(half):
            return slice(0, N) if half is None else slice(half * P, (half + 1) * P)

        block = ctx.enter_context(nc.Block())

        @block.sync
        def _(sp):
            def load_ids(i, u):
                sp.dma_start(idx[:, u, :], ids_fetched[bass.ds(i * N + u * P, P), :])\
                    .then_inc(ids_in[u], 16)

            def load_ids_b(i):
                sp.dma_start(ids_b[:, :, :], ids_selected[:, bass.ds(i * N, N)]
                             .rearrange("(a t) n -> a t n", a=1).to_broadcast([CR, NS, N]))\
                    .then_inc(ids_b_in, 16)

            def load_dense(i):
                sp.dma_start(staged[:, 0, :], dense_t[:, bass.ds(i * N, N)]).then_inc(staged_in, 16)

            def load_zt(i):
                sp.dma_start(zt[:, ZC, :], dense_t[:, bass.ds(i * N, N)]).then_inc(zt_in, 16)

            load_ids(0, 0)
            load_ids_b(0)
            for o in range(NS):
                sp.dma_start(rest[:, o, :], tables[SELECTED[o]].rearrange("(r c) d -> r (c d)", c=CHUNKS))\
                    .then_inc(table_in[o], 16)
                if o == 0:
                    load_ids(0, 1)
            load_dense(0)
            load_zt(0)
            sp.wait_ge(ids_s_done, 1)
            load_ids_b(1)
            sp.wait_ge(rows_in[0][NG // 2], 16 * (GROUPS[NG // 2][1] - GROUPS[NG // 2][0]))
            sp.dma_start(w1ab[:, :, :], w1_dense.rearrange("a k n -> k a n")).then_inc(w1ab_in, 16)
            sp.dma_start(w1z[:, :, :], w1_pairs.rearrange("(c k) n -> k c n", c=ZC)).then_inc(w1z_in, 16)
            sp.dma_start(w2s[:, :, :], w2.rearrange("(c k) n -> k c n", c=C1)).then_inc(mlp_in, 16)
            sp.dma_start(w3s[:, :], w3).then_inc(mlp_in, 16)
            sp.dma_start(b1s[:, :], b1).then_inc(mlp_in, 16)
            sp.dma_start(b2s[:, :], b2).then_inc(mlp_in, 16)

            last_group = 16 * (GROUPS[-1][1] - GROUPS[-1][0])

            def next_ids(i, u):
                sp.wait_ge(rows_in[u][NG - 1], i * last_group + last_group)
                sp.sem_inc(sp_passed, 1)
                load_ids(i + 1, u)

            def next_dense(i):
                sp.wait_ge(staged_taken, i * 2 + 2)
                sp.sem_inc(sp_passed, 1)
                load_dense(i + 1)

            def next_ids_b(i):
                sp.wait_ge(ids_s_done, i + 2)
                sp.sem_inc(sp_passed, 1)
                load_ids_b(i + 2)

            def pair(i):
                next_ids(i, 0)
                next_dense(i)
                next_ids(i, 1)
                sp.wait_ge(layer, i * MLPS - (MLPS - C1))
                sp.sem_inc(sp_passed, 1)
                load_zt(i)

            next_ids(0, 0)
            next_dense(0)
            next_ids(0, 1)
            next_ids_b(0)
            with sp.Fori(1, NP - 2) as i:
                pair(i)
                next_ids_b(i)
            pair(NP - 2)
            sp.wait_ge(layer, (NP - 2) * MLPS + C1)
            load_zt(NP - 1)
            sp.wait_ge(layer_taken, (NP + 1) * MLPS + 1)
            sp.dma_start(out.rearrange("b a -> a b"), y[:, :]).then_inc(y_out, 16)
            sp.wait_ge(y_out, 16)

        @block.gpsimd
        def _(pool):
            pool.memset(ident[:, :], 0.0).then_inc(ident_zero, 1)
            pool.wait_ge(ident_zero, 1)
            pool.affine_select(out=ident[:, :], in_=ident[:, :], compare_op=ALU.not_equal, fill=1.0,
                               base=0, pattern=[[-1, P]], channel_multiplier=1).then_inc(ident_done, 1)
            pool.iota(row_i[:, :], pattern=[[1, CHUNKS]], base=0, channel_multiplier=CHUNKS)\
                .then_inc(row_i_done, 1)
            with pool.Fori(0, NP) as i:
                for u in range(2):
                    pool.wait_ge(ids_in[u], i * 16 + 16)
                    pool.sem_inc(pool_passed, 1)
                    for g, (a, b) in enumerate(GROUPS):
                        pool.wait_ge(turned, i * (2 * TURNS) + (u * TURNS + g + SKIPPED + 1))
                        pool.sem_inc(pool_passed, 1)
                        for s in range(a, b):
                            n = s - S0
                            pool.indirect_dma_start(
                                rows[:, u, n, :], None, tables[FETCHED[n]],
                                bass.IndirectOffsetOnAxis(ap=idx[:, u, n:n + 1], axis=0))\
                                .then_inc(rows_in[u][g], 16)

        @block.tensor
        def _(pe):
            def turn_rows(i, u, g, first=False):
                a, b = GROUPS[g]
                bank = turn_bank(u, g, first)
                pe.wait_ge(rows_in[u][g], i * (16 * (b - a)) + 16 * (b - a))
                pe.wait_ge(turn_taken, group_turn(i, u, g) + 1)
                for s in range(a, b):
                    t = pe.transpose(turn_ps[:, bank, (s - a) * P:(s - a + 1) * P],
                                     rows[:, u, s - S0, :], ident[:, :])
                t.then_inc(turned, 1)

            def gram_blocks(i, u, c):
                if c == 0:
                    pe.wait_ge(turn_taken, group_turn(i, u, NG - 1) + (BANKS + 1))
                    pe.wait_ge(staged_taken, i * 2 + (u + 1))
                pe.wait_ge(gram_taken, i * (2 * GRAMS) + (u * GRAMS + c + 1))
                for k in range(GB):
                    j = c * GB + k
                    m = pe.matmul(gram_ps[:, c % 2, k * P:k * P + QUADS * F]
                                  .rearrange("p (s g) -> p s g", s=QUADS),
                                  feat[:, u, j * QUADS:(j + 1) * QUADS, :].rearrange("d s f -> d (s f)"),
                                  feat[:, u, j * QUADS:(j + 1) * QUADS, 0:F],
                                  start=True, stop=True)
                m.then_inc(grammed, 1)

            def turn_pairs(i, u, last=False):
                pe.wait_ge(pairs_done, i * 2 + (u + 1))
                pe.wait_ge(turn_taken, pairs_turn(i, u, last) + 1)
                flat = pairs[:, u, :, :].rearrange("p k f -> p (k f)")
                for c in range(ZC):
                    t = pe.transpose(turn_ps[0:ZK, pairs_bank(u, last), c * P:(c + 1) * P],
                                     flat[:, c * ZK:(c + 1) * ZK], ident[:, :])
                t.then_inc(turned, 1)

            def pick(i, o):
                pe.wait_ge(onehot_done, i * NS + (o + 1))
                pe.wait_ge(pick_taken, i * NS + (o + 1))
                for c in range(CHUNKS):
                    for q in range(PARTS):
                        m = pe.matmul(pick_ps, parts[:, o, q, c * D:(c + 1) * D],
                                      onehot[:, o, c, :], start=(c == 0 and q == 0),
                                      stop=(c == CHUNKS - 1 and q == PARTS - 1))
                m.then_inc(picked, 1)

            def mlp(i, n, half=None, two=False, last=False):
                number = layer_number(i, n, half)
                ps = layer_bank(number, two)
                x = columns(half)
                if two and n > 0:
                    pe.wait_ge(layer_taken, number)
                else:
                    pe.wait_ge(layer_taken, number + 1)
                if n == 0:
                    pe.wait_ge(turn_taken, pairs_turn(i, 0 if half == 0 else 1, last) + (BANKS + 1))
                    pe.wait_ge(zt_in, i * 16 + 16)
                if n < C1:
                    for c in range(ZC):
                        pe.matmul(ps[:, x], w1z[:, c, n * P:(n + 1) * P], zt[0:ZK, c, x],
                                  start=(c == 0), stop=False)
                    h = pe.matmul(ps[:, x], w1d[:, n * P:(n + 1) * P], zt[:, ZC, x],
                                  start=False, stop=True)
                elif n < C1 + C2:
                    m = n - C1
                    for c in range(C1):
                        if two and m == 0:
                            pe.wait_ge(layer_taken, layer_number(i, c, half) + 2)
                        h = pe.matmul(ps[:, x], w2s[:, c, m * P:(m + 1) * P], h1[:, c, x],
                                      start=(c == 0), stop=(c == C1 - 1))
                else:
                    for c in range(C2):
                        if two:
                            pe.wait_ge(layer_taken, layer_number(i, C1 + c, half) + 2)
                        h = pe.matmul(ps[0:1, x], w3s[:, c:c + 1], h2[:, c, x],
                                      start=(c == 0), stop=(c == C2 - 1))
                h.then_inc(layer, 1)

            pe.sem_inc(turned, rows_free + SKIPPED)
            pe.wait_ge(ident_done, 1)
            order = part_order()
            for o in range(NS):
                pe.wait_ge(act_part, order.index((PARTS - 1, o)) + 1)
                pick(0, o)
                if NS - BANKS - 1 <= o < NS - 1:
                    turn_rows(0, 0, o + 1 + BANKS - NS, first=True)
            for g in range(BANKS, NG):
                turn_rows(0, 0, g, first=True)

            def pair(i, first=False, last=False):
                for c in range(GRAMS):
                    gram_blocks(i, 0, c)
                    if c == 1 and not first:
                        turn_pairs(i - 1, 1)
                    if c > 1 and not first:
                        mlp(i - 1, c - 2, two=last)
                    turn_rows(i, 1, c, first)
                if not last:
                    pick(i + 1, 0)
                if not first:
                    mlp(i - 1, 2, two=last)
                if last:
                    turn_rows(i, 1, GRAMS)
                    for n in range(C1 - 1, MLPS):
                        mlp(i - 1, n, two=last)
                for g in range(GRAMS + last, NG):
                    turn_rows(i, 1, g, first)
                if not first and not last:
                    mlp(i - 1, C1 - 1)
                for c in range(GRAMS):
                    gram_blocks(i, 1, c)
                    if c == 1:
                        turn_pairs(i, 0, last)
                    if not last and c + 1 < NS:
                        pick(i + 1, c + 1)
                    if c == 2 and not first and not last:
                        mlp(i - 1, C1)
                    if not last:
                        turn_rows(i + 1, 0, c)
                if not last:
                    if not first:
                        mlp(i - 1, C1 + 1)
                    for g in range(GRAMS, NG):
                        turn_rows(i + 1, 0, g)
                    if not first:
                        mlp(i - 1, C1 + 2)

            pair(0, first=True)
            pe.wait_ge(w1z_in, 16)
            pe.wait_ge(w1d_done, 1)
            pe.wait_ge(mlp_in, 64)
            with pe.Fori(1, NP - 1) as i:
                pair(i)
            pair(NP - 1, last=True)
            for n in range(C1):
                mlp(NP - 1, n, half=0, two=True, last=True)
            turn_pairs(NP - 1, 1, last=True)
            for n in range(C1, MLPS):
                mlp(NP - 1, n, half=0, two=True, last=True)
            for n in range(MLPS):
                mlp(NP - 1, n, half=1, two=True, last=True)

        @block.vector
        def _(dve):
            def convert_ids(i):
                dve.wait_ge(ids_b_in, i * 16 + 16)
                dve.tensor_copy(ids_s[:, :, :], ids_b[:, :, :]).then_inc(ids_s_done, 1)

            def make_onehot(i, o, first=False):
                dve.wait_ge(ids_s_done, i + 1)
                if not first:
                    dve.wait_ge(picked, i * NS - (NS - o - 1))
                for c in range(CHUNKS):
                    t = dve.tensor_scalar(onehot[:, o, c, :], ids_s[:, o, :], row_id[:, c:c + 1],
                                          None, ALU.is_equal)
                t.then_inc(onehot_done, 1)

            def place_staged(i, u):
                dve.wait_ge(pick_taken, i * NS + (NS + 1))
                dve.wait_ge(staged_in, i * 16 + 16)
                dve.tensor_copy(feat[:, u, :, 0:S0].rearrange("d p s -> d s p"),
                                staged[:, :, u * P:(u + 1) * P]).then_inc(staged_taken, 1)

            def place_rows(i, u, g, first=False):
                a, b = GROUPS[g]
                dve.wait_ge(turned, group_turn(i, u, g) + (rows_free + 1))
                dve.tensor_copy(feat[:, u, :, a:b].rearrange("d p s -> d s p"),
                                turn_ps[:, turn_bank(u, g, first), 0:(b - a) * P]
                                .rearrange("d (s p) -> d s p", p=P)).then_inc(turn_taken, 1)

            def make_z(i, u):
                dve.wait_ge(gram_taken, i * (2 * GRAMS) + ((u + 1) * GRAMS + 2))
                dve.transpose(z[:, u, 0:F, :], gram[:, u, :, :])
                dve.transpose(z[:, u, F:F + K_MAX, :], gram[:, u, 0:K_MAX, :]).then_inc(z_done, 1)
                dve.wait_ge(z_done, i * 2 + (u + 3))
                flat = z[:, u, :, :].rearrange("p g f -> p (g f)")
                diagonals = bass.AP(flat.tensor, flat.offset + SUB,
                                    [list(flat.ap[0]), [SUB, K_MAX], [SUB + 1, F]])
                dve.tensor_copy(pairs[:, u, :, :], diagonals).then_inc(pairs_done, 1)

            def place_pairs(i, u, last=False):
                dve.wait_ge(turned, pairs_turn(i, u, last) + (rows_free + 1))
                dve.tensor_copy(zt[0:ZK, 0:ZC, u * P:(u + 1) * P].rearrange("k c (j s) -> k c s j", s=QUADS),
                                turn_ps[0:ZK, pairs_bank(u, last), 0:ZC * P]
                                .rearrange("k (c s j) -> k c s j", c=ZC, s=QUADS))\
                    .then_inc(turn_taken, 1)

            dve.sem_inc(turn_taken, BANKS + SKIPPED)
            dve.sem_inc(z_done, 2)
            for u in range(2):
                dve.memset(feat[:, u, :, F:SUB], 0.0).then_inc(feat_zero, 1)
            dve.wait_ge(row_i_done, 1)
            dve.tensor_copy(row_id[:, :], row_i[:, :]).then_inc(row_id_done, 1)
            dve.wait_ge(row_id_done, 1)
            convert_ids(0)
            for n, (q, o) in enumerate(part_order()):
                if q == 0:
                    make_onehot(0, o, first=True)
                if q < PARTS - 1:
                    dve.wait_ge(act_part, n + 1)
                    dve.tensor_tensor(rest[:, o, :], rest[:, o, :], parts[:, o, q, :], ALU.subtract)\
                        .then_inc(dve_rest, 1)
            for g in range(NG):
                place_rows(0, 0, g, first=True)
            place_staged(0, 0)

            def pair(i, first=False, last=False):
                place_staged(i, 1)
                if not last:
                    convert_ids(i + 1)
                for c in range(GRAMS):
                    if c == 1 and not first:
                        place_pairs(i - 1, 1)
                    place_rows(i, 1, c, first)
                    if not last and c < min(NS, GRAMS - 1):
                        make_onehot(i + 1, c)
                make_z(i, 0)
                for g in range(GRAMS, NG):
                    place_rows(i, 1, g, first)
                if not last:
                    for o in range(GRAMS - 1, NS):
                        make_onehot(i + 1, o)
                if first:
                    dve.wait_ge(w1ab_in, 16)
                    dve.tensor_tensor(w1d[:, :], w1ab[:, 0, :], w1ab[:, 1, :], ALU.add).then_inc(w1d_done, 1)
                for c in range(GRAMS):
                    if c == 1:
                        place_pairs(i, 0, last)
                    if not last:
                        place_rows(i + 1, 0, c)
                if not last:
                    place_staged(i + 1, 0)
                    for g in range(GRAMS, NG):
                        place_rows(i + 1, 0, g)
                make_z(i, 1)

            pair(0, first=True)
            with dve.Fori(1, NP - 1) as i:
                pair(i)
            pair(NP - 1, last=True)
            place_pairs(NP - 1, 1, last=True)

        @block.scalar
        def _(act):
            def keep_grams(i, u, c):
                if c == 0:
                    act.wait_ge(z_done, i * 2 + (u + 1))
                act.wait_ge(grammed, i * (2 * GRAMS) + (u * GRAMS + c + 1))
                blocks = gram_ps[:, c % 2, :].rearrange("p (j x) -> p j x", j=GB)
                for s in range(QUADS):
                    q = slice(s * SUB, (s + 1) * SUB)
                    t = act.activation(gram[q, u, :, c * GB:(c + 1) * GB].rearrange("p g j -> p j g"),
                                       blocks[q, :, s * F:(s + 1) * F], ACT.Copy)
                t.then_inc(gram_taken, 1)

            def keep_pick(i, o):
                act.wait_ge(picked, i * NS + (o + 1))
                act.activation(staged[:, 1 + o, :], pick_ps, ACT.Copy).then_inc(pick_taken, 1)

            def keep_mlp(i, n, half=None, two=False):
                number = layer_number(i, n, half)
                ps = layer_bank(number, two)
                x = columns(half)
                act.wait_ge(layer, number + 1)
                if n < C1:
                    t = act.activation(h1[:, n, x], ps[:, x], ACT.Relu, bias=b1s[:, n:n + 1])
                elif n < C1 + C2:
                    m = n - C1
                    t = act.activation(h2[:, m, x], ps[:, x], ACT.Relu, bias=b2s[:, m:m + 1])
                else:
                    t = act.activation(y[:, bass.ds(i * N + x.start, x.stop - x.start)], ps[0:1, x], ACT.Copy)
                t.then_inc(layer_taken, 1)

            act.sem_inc(gram_taken, 2)
            act.sem_inc(pick_taken, 1)
            act.sem_inc(layer_taken, 1)
            order = part_order()
            taken_off = [x for x in order if x[0] < PARTS - 1]
            for q, o in order:
                if q == 0:
                    act.wait_ge(table_in[o], 16)
                else:
                    act.wait_ge(dve_rest, taken_off.index((q - 1, o)) + 1)
                act.activation(parts[:, o, q, :], rest[:, o, :], ACT.Copy).then_inc(act_part, 1)
                if q == PARTS - 1 and o > 0:
                    keep_pick(0, o - 1)
            keep_pick(0, NS - 1)

            def pair(i, first=False, last=False):
                for c in range(GRAMS):
                    keep_grams(i, 0, c)
                    if c > 1 and not first:
                        keep_mlp(i - 1, c - 2, two=last)
                if not last:
                    act.wait_ge(staged_taken, i * 2 + 2)
                    keep_pick(i + 1, 0)
                if not first:
                    for n in range(2, MLPS if last else C1):
                        keep_mlp(i - 1, n, two=last)
                for c in range(GRAMS):
                    keep_grams(i, 1, c)
                    if not last and c + 1 < NS:
                        keep_pick(i + 1, c + 1)
                    if c == 2 and not first and not last:
                        keep_mlp(i - 1, C1)
                if not first and not last:
                    keep_mlp(i - 1, C1 + 1)
                    keep_mlp(i - 1, C1 + 2)

            pair(0, first=True)
            act.wait_ge(mlp_in, 64)
            with act.Fori(1, NP - 1) as i:
                pair(i)
            pair(NP - 1, last=True)
            for half in range(2):
                for n in range(MLPS):
                    keep_mlp(NP - 1, n, half=half, two=True)


def kernel(**inputs):
    import numpy as np
    import concourse.bacc as bacc
    from concourse.bass_utils import run_bass_kernel_spmd as run

    a = {k: np.asarray(v) for k, v in inputs.items()}
    ids, w1 = a["ids"], a["W_top1"]
    arrays = {
        "dense_t": a["r_dense_output"].T,
        "ids_fetched": ids[:, FETCHED],
        "ids_selected": ids[:, SELECTED].T,
        "w1_pairs": w1[pair_rows()],
        "w1_dense": np.stack([w1[:D], w1[D + PAIRS:]]),
        "w2": a["W_top2"],
        "w3": a["W_top3"].reshape(-1, P).T,
        "b1": a["b_top1"].reshape(-1, P).T,
        "b2": a["b_top2"].reshape(-1, P).T,
    }
    arrays |= {f"tbl_{f}": a[f"tbl_{f}"] for f in range(len(TABLE_ROWS))}
    arrays = {k: np.ascontiguousarray(v) for k, v in arrays.items()}

    nc = bacc.Bacc("TRN2", target_bir_lowering=False, num_devices=1)
    ap = {k: nc.dram_tensor(k, v.shape, mybir.dt.from_np(v.dtype), kind="ExternalInput").ap()
          for k, v in arrays.items()}
    out = nc.dram_tensor("y_out_dram", (ids.shape[0], 1), F32, kind="ExternalOutput").ap()
    tower(nc, ap["dense_t"], ap["ids_fetched"], ap["ids_selected"],
          [ap[f"tbl_{f}"] for f in range(len(TABLE_ROWS))], ap["w1_pairs"], ap["w1_dense"],
          ap["w2"], ap["w3"], ap["b1"], ap["b2"], out)
    return run(nc, [arrays], core_ids=[0]).results[0]["y_out_dram"]
```

```python
from contextlib import ExitStack

import concourse.bass as bass
from concourse import mybir

F32 = mybir.dt.float32
F32R = mybir.dt.float32r
U32 = mybir.dt.uint32
F16 = mybir.dt.float16
I32 = mybir.dt.int32
ALU = mybir.AluOpType
ACT = mybir.ActivationFunctionType

P = 128
D = 128
TABLE_ROWS = [1000, 1250, 12500, 1250, 125000, 1250, 12500, 1000, 1000, 1250, 1000, 12500, 1250,
              12500, 1000, 1250, 12500, 1000, 1000, 1000, 12500, 1250, 1000, 1000, 1250, 1000]
SELECTED = [0, 7, 8, 10, 14, 17, 18]
FETCHED = [f for f in range(len(TABLE_ROWS)) if f not in SELECTED]
SLOTS = [0] + [1 + f for f in SELECTED] + [1 + f for f in FETCHED]
LATE = SELECTED[5:]
F = len(SLOTS)
K_MAX = (F - 1) // 2
PAIRS = F * (F - 1) // 2
ZC = 3
ZK = PAIRS // ZC
SUB = 32
QUADS = P // SUB
GM = P - SUB + F
ROWS = 1000
CHUNKS = 8
CR = ROWS // CHUNKS
PARTS = 2
LEADING = 0xFFFFF000
STAGES = 4
RING = 3
NS = len(SELECTED)
NL = len(LATE)
NE = NS - NL
NF = len(FETCHED)
S0 = 1 + NS
GROUP_SIZES = [4, 4, 4, 4, 2, 1]
GROUPS = [(S0 + sum(GROUP_SIZES[:g]), S0 + sum(GROUP_SIZES[:g + 1])) for g in range(len(GROUP_SIZES))]
NG = len(GROUPS)
assert GROUPS[-1][1] == F
GRAMS = 4
GB = SUB // GRAMS
TURNS = NG + 1
SKIPPED = 2
BANKS = 2


def group_turn(i, u, g):
    if isinstance(i, int) and i == 0:
        return SKIPPED + u * NG + g
    return i * (2 * TURNS) + (u * TURNS + (g + 1 if g else 0))


def pairs_turn(i, u, last=False):
    return i * (2 * TURNS) + (2 * TURNS + u if last else (u + 2) * TURNS + 1)


def turn_bank(u, g, first):
    return group_turn(0, u, g) % BANKS if first else (u * TURNS + (g + 1 if g else 0)) % BANKS


def pairs_bank(u, last):
    return pairs_turn(0, u, last) % BANKS


def pair_rows():
    first = {}
    n = D
    for a in range(F):
        for b in range(a + 1, F):
            first[a, b] = n
            n += 1
    rows = []
    for k in range(1, K_MAX + 1):
        for f in range(F):
            a, b = SLOTS[f], SLOTS[(f + k) % F]
            rows.append(first[min(a, b), max(a, b)])
    return rows


def tower(nc, dense_t, ids_fetched, ids_selected, tables, w1_pairs, w1_dense, w2, w3, b1, b2, out):
    B = dense_t.shape[1]
    H1 = w1_dense.shape[2]
    H2 = w2.shape[1]
    C1 = H1 // P
    N = 2 * P
    NP = B // N
    ROW = CHUNKS * D
    assert (C1, GRAMS, NG, NS, NL) == (4, 4, 6, 7, 2)

    with ExitStack() as ctx:
        def sb(name, shape, dt):
            return ctx.enter_context(nc.sbuf_tensor(name, shape, dt))

        def psum(name, shape):
            return ctx.enter_context(nc.psum_tensor(name, shape, F32))

        def sem(name):
            return ctx.enter_context(nc.semaphore(name))

        ident = sb("ident", [P, P], F32)
        row_i = sb("row_i", [CR, 1], I32)
        row_id = sb("row_id", [CR, 1], F32)
        w1z = sb("w1z", [ZK, ZC, H1], F32)
        w1ab = sb("w1ab", [P, 2, H1], F32)
        w1d = sb("w1d", [P, H1], F32)
        w2s = sb("w2s", [P, C1, H2], F32)
        b1s = sb("b1s", [P, C1], F32)
        w3s = sb("w3s", [P, H2], F32)
        b2s = sb("b2s", [P, H2], F32)
        parts = sb("parts", [CR, NS, PARTS, ROW], F32R)
        idx = sb("idx", [P, 2, NF + NL], I32)
        late_rows = sb("late_rows", [P, 2, NL, D], F32)
        rows = sb("rows", [P, 2, NF, D], F32)
        ids_b = sb("ids_b", [CR, NS, N], I32)
        ids_s = sb("ids_s", [CR, NS, N], F16)
        onehot = sb("onehot", [CR, RING, CHUNKS, N], F32R)
        staged = sb("staged", [P, S0, N], F32)
        feat = sb("feat", [P, 2, P, SUB], F32)
        gram = sb("gram", [P, 2, F, SUB], F32)
        z = sb("z", [P, 2, F + K_MAX, SUB], F32)
        pairs = sb("pairs", [P, 2, K_MAX, F], F32)
        zt = sb("zt", [P, ZC + 1, N], F32)
        h1 = sb("h1", [P, C1, N], F32)
        h2 = sb("h2", [P, 2, H2], F32)
        h2w = sb("h2w", [P, 2, H2], F32)
        y = sb("y", [P, B // P], F32)
        yt = sb("yt", [B // P, P], F32)
        staging = feat[0:CR, 1, :, :].rearrange("p s f -> p (s f)")
        tables_s = [staging[:, k * ROW:(k + 1) * ROW] for k in range(STAGES)]
        leading = [z[0:CR, :, :, :].rearrange("p u g f -> p (u g f)")[:, k * ROW:(k + 1) * ROW]
                   for k in range(2)]

        turn_ps = psum("turn_ps", [P, 2, 512])
        gram_ps = psum("gram_ps", [P, 2, GB * P])
        pick_bank = psum("pick_ps", [P, 512])
        pick_ps = pick_bank[:, 0:N]
        mlp_ps = psum("mlp_ps", [P, 512])[:, 0:N]

        ids_in = [sem(f"ids_in{u}") for u in range(2)]
        rows_in = [[sem(f"rows_in{u}_{g}") for g in range(NG)] for u in range(2)]
        late_in = [sem(f"late_in{u}") for u in range(2)]
        ids_b_in = sem("ids_b_in")
        staged_in = sem("staged_in")
        zt_in = sem("zt_in")
        table_in = [sem(f"table_in{o}") for o in range(NS)]
        w1z_in = sem("w1z_in")
        w1ab_in = sem("w1ab_in")
        mlp_in = sem("mlp_in")
        y_out = sem("y_out")
        pool_passed = sem("pool_passed")
        sp_passed = sem("sp_passed")
        ident_zero = sem("ident_zero")
        ident_done = sem("ident_done")
        row_i_done = sem("row_i_done")
        row_id_done = sem("row_id_done")
        feat_zero = sem("feat_zero")
        w1d_done = sem("w1d_done")
        leading_done = sem("leading_done")
        high_done = sem("high_done")
        low_done = sem("low_done")
        late_turned = sem("late_turned")
        late_taken = sem("late_taken")
        turned = sem("turned")
        turn_taken = sem("turn_taken")
        staged_taken = sem("staged_taken")
        ids_s_done = sem("ids_s_done")
        onehot_done = sem("onehot_done")
        picked = sem("picked")
        pick_taken = sem("pick_taken")
        grammed = sem("grammed")
        gram_taken = sem("gram_taken")
        z_done = sem("z_done")
        pairs_done = sem("pairs_done")
        hidden = sem("hidden")
        hidden_taken = sem("hidden_taken")
        second = sem("second")
        second_taken = sem("second_taken")
        scored = sem("scored")
        y_turned = sem("y_turned")
        yt_done = sem("yt_done")
        rows_free = TURNS * 2

        def columns(half):
            return slice(0, N) if half is None else slice(half * P, (half + 1) * P)

        block = ctx.enter_context(nc.Block())

        @block.sync
        def _(sp):
            def load_ids(i, u):
                sp.dma_start(idx[:, u, :], ids_fetched[bass.ds(i * N + u * P, P), :])\
                    .then_inc(ids_in[u], 16)

            def load_ids_b(i):
                sp.dma_start(ids_b[:, :, :], ids_selected[:, bass.ds(i * N, N)]
                             .rearrange("(a t) n -> a t n", a=1).to_broadcast([CR, NS, N]))\
                    .then_inc(ids_b_in, 16)

            def load_dense(i):
                sp.dma_start(staged[:, 0, :], dense_t[:, bass.ds(i * N, N)]).then_inc(staged_in, 16)

            def load_zt(i):
                sp.dma_start(zt[:, ZC, :], dense_t[:, bass.ds(i * N, N)]).then_inc(zt_in, 16)

            def load_table(o):
                sp.dma_start(tables_s[o % STAGES], tables[SELECTED[o]].rearrange("(r c) d -> r (c d)", c=CHUNKS))\
                    .then_inc(table_in[o], 16)

            load_ids(0, 0)
            load_table(0)
            load_ids_b(0)
            load_table(1)
            load_ids(0, 1)
            for o in range(2, STAGES):
                load_table(o)
            load_dense(0)
            load_zt(0)
            for o in range(STAGES, NS):
                sp.wait_ge(low_done, o - STAGES + 1)
                load_table(o)
            sp.wait_ge(ids_s_done, 1)
            load_ids_b(1)

            last_group = 16 * (GROUPS[-1][1] - GROUPS[-1][0])

            def next_ids(i, u):
                sp.wait_ge(rows_in[u][NG - 1], i * last_group + last_group)
                sp.sem_inc(sp_passed, 1)
                load_ids(i + 1, u)

            def next_dense(i):
                sp.wait_ge(staged_taken, i * 2 + 2)
                sp.sem_inc(sp_passed, 1)
                load_dense(i + 1)

            def next_ids_b(i):
                sp.wait_ge(ids_s_done, i + 2)
                sp.sem_inc(sp_passed, 1)
                load_ids_b(i + 2)

            def pair(i):
                next_ids(i, 0)
                next_dense(i)
                next_ids(i, 1)
                sp.wait_ge(hidden, i * C1)
                sp.sem_inc(sp_passed, 1)
                load_zt(i)

            def after_rows(i, u, g):
                sp.wait_ge(rows_in[u][g], (i + 1) * 16 * (GROUPS[g][1] - GROUPS[g][0]))

            def load_w1z(c):
                sp.dma_start(w1z[:, c, :], w1_pairs[c * ZK:(c + 1) * ZK, :]).then_inc(w1z_in, 16)

            def load_w2(half):
                c = slice(half * C1 // 2, (half + 1) * C1 // 2)
                sp.dma_start(w2s[:, c, :], w2.rearrange("(c k) n -> k c n", c=C1)[:, c, :]).then_inc(mlp_in, 16)

            next_ids(0, 0)
            next_dense(0)
            after_rows(0, 1, 0)
            load_w1z(0)
            after_rows(0, 1, 1)
            load_w1z(1)
            after_rows(0, 1, 2)
            load_w1z(2)
            next_ids(0, 1)
            sp.dma_start(w1ab[:, 0, :], w1_dense[0]).then_inc(w1ab_in, 16)
            after_rows(1, 0, 0)
            sp.dma_start(w1ab[:, 1, :], w1_dense[1]).then_inc(w1ab_in, 16)
            after_rows(1, 0, 1)
            load_w2(0)
            sp.dma_start(b1s[:, :], b1).then_inc(mlp_in, 16)
            after_rows(1, 0, 2)
            load_w2(1)
            after_rows(1, 0, 3)
            sp.dma_start(w3s[:, :], w3.to_broadcast([P, H2])).then_inc(mlp_in, 16)
            sp.dma_start(b2s[:, :], b2.to_broadcast([P, H2])).then_inc(mlp_in, 16)
            next_ids_b(0)
            with sp.Fori(1, NP - 2) as i:
                pair(i)
                next_ids_b(i)
            pair(NP - 2)
            sp.wait_ge(hidden, (NP - 1) * C1)
            load_zt(NP - 1)
            sp.wait_ge(yt_done, 1)
            sp.dma_start(out.rearrange("(t p) a -> t (p a)", p=P), yt[:, :]).then_inc(y_out, 16)
            sp.wait_ge(y_out, 16)

        @block.gpsimd
        def _(pool):
            pool.memset(ident[:, :], 0.0).then_inc(ident_zero, 1)
            pool.wait_ge(ident_zero, 1)
            pool.affine_select(out=ident[:, :], in_=ident[:, :], compare_op=ALU.not_equal, fill=1.0,
                               base=0, pattern=[[-1, P]], channel_multiplier=1).then_inc(ident_done, 1)
            pool.iota(row_i[:, :], pattern=[[0, 1]], base=0, channel_multiplier=CHUNKS)\
                .then_inc(row_i_done, 1)

            def fetch(to, u, n, table, landed):
                pool.indirect_dma_start(to, None, tables[table],
                                        bass.IndirectOffsetOnAxis(ap=idx[:, u, n:n + 1], axis=0))\
                    .then_inc(landed, 16)

            def fetch_tile(i, u, first=False, last=False):
                pool.wait_ge(ids_in[u], i * 16 + 16)
                if not first and not last:
                    pool.sem_inc(pool_passed, 1)
                if last:
                    for n in range(NL):
                        fetch(late_rows[:, u, n, :], u, NF + n, LATE[n], late_in[u])
                for g, (a, b) in enumerate(GROUPS):
                    if not first:
                        pool.wait_ge(turned, i * (2 * TURNS) + (u * TURNS + g + SKIPPED + 1))
                        if not last:
                            pool.sem_inc(pool_passed, 1)
                    for s in range(a, b):
                        fetch(rows[:, u, s - S0, :], u, s - S0, FETCHED[s - S0], rows_in[u][g])

            for u in range(2):
                fetch_tile(0, u, first=True)
            with pool.Fori(1, NP - 1) as i:
                for u in range(2):
                    fetch_tile(i, u)
            for u in range(2):
                fetch_tile(NP - 1, u, last=True)

        @block.tensor
        def _(pe):
            def turn_rows(i, u, g, first=False):
                a, b = GROUPS[g]
                bank = turn_bank(u, g, first)
                pe.wait_ge(rows_in[u][g], i * (16 * (b - a)) + 16 * (b - a))
                pe.wait_ge(turn_taken, group_turn(i, u, g) + 1)
                for s in range(a, b):
                    t = pe.transpose(turn_ps[:, bank, (s - a) * P:(s - a + 1) * P],
                                     rows[:, u, s - S0, :], ident[:, :])
                t.then_inc(turned, 1)

            def gram_blocks(i, u, c, last=False):
                if c == 0:
                    pe.wait_ge(turn_taken, group_turn(i, u, NG - 1) + (BANKS + 1))
                    pe.wait_ge(staged_taken, i * 2 + (u + 1))
                    if last:
                        pe.wait_ge(late_taken, u + 1)
                pe.wait_ge(gram_taken, i * (2 * GRAMS) + (u * GRAMS + c + 1))
                for k in range(GB):
                    j = c * GB + k
                    m = pe.matmul(gram_ps[0:GM, c % 2, k * P:k * P + QUADS * F]
                                  .rearrange("p (s g) -> p s g", s=QUADS),
                                  feat[:, u, j * QUADS:(j + 1) * QUADS, :].rearrange("d s f -> d (s f)")[:, 0:GM],
                                  feat[:, u, j * QUADS:(j + 1) * QUADS, 0:F],
                                  start=True, stop=True)
                m.then_inc(grammed, 1)

            def turn_pairs(i, u, last=False):
                pe.wait_ge(pairs_done, i * 2 + (u + 1))
                pe.wait_ge(turn_taken, pairs_turn(i, u, last) + 1)
                flat = pairs[:, u, :, :].rearrange("p k f -> p (k f)")
                for c in range(ZC):
                    t = pe.transpose(turn_ps[0:ZK, pairs_bank(u, last), c * P:(c + 1) * P],
                                     flat[:, c * ZK:(c + 1) * ZK], ident[:, :])
                t.then_inc(turned, 1)

            def pick(i, o):
                pe.wait_ge(onehot_done, i * NS + (o + 1))
                pe.wait_ge(pick_taken, i * NS + (o + 1))
                for c in range(CHUNKS):
                    for q in range(PARTS):
                        m = pe.matmul(pick_ps, parts[:, o, q, c * D:(c + 1) * D],
                                      onehot[:, o % RING, c, :], start=(c == 0 and q == 0),
                                      stop=(c == CHUNKS - 1 and q == PARTS - 1))
                m.then_inc(picked, 1)

            def layer1(i, n, ps=mlp_ps, half=None, last=False):
                x = columns(half)
                if n == 0:
                    pe.wait_ge(turn_taken, pairs_turn(i, 0 if half == 0 else 1, last) + (BANKS + 1))
                    pe.wait_ge(zt_in, i * 16 + 16)
                for c in range(ZC):
                    pe.matmul(ps[:, x], w1z[:, c, n * P:(n + 1) * P], zt[0:ZK, c, x],
                              start=(c == 0), stop=False)
                pe.matmul(ps[:, x], w1d[:, n * P:(n + 1) * P], zt[:, ZC, x],
                          start=False, stop=True).then_inc(hidden, 1)

            def layer1_in_turn(i, n):
                if n == 0:
                    pe.wait_ge(second_taken, i * 2 + 1)
                else:
                    pe.wait_ge(hidden_taken, i * C1 + n)
                layer1(i, n)

            def layer2(i, u, ps=mlp_ps, taken=None):
                for c in range(C1):
                    if taken is not None:
                        pe.wait_ge(hidden_taken, taken - (C1 - 1 - c))
                    m = pe.matmul(ps, h1[:, c, u * P:(u + 1) * P], w2s[:, c, :],
                                  start=(c == 0), stop=(c == C1 - 1))
                m.then_inc(second, 1)

            def layer2_in_turn(i, u):
                if u == 0:
                    pe.wait_ge(hidden_taken, i * C1 + C1)
                else:
                    pe.wait_ge(second_taken, i * 2 + 2)
                layer2(i, u)

            def turn_late(u):
                pe.wait_ge(late_in[u], 16 * NL)
                if u == 0:
                    pe.wait_ge(pick_taken, (NP - 1) * NS + (NE + 1))
                else:
                    pe.wait_ge(late_taken, u)
                for n in range(NL):
                    t = pe.transpose(pick_bank[:, n * P:(n + 1) * P], late_rows[:, u, n, :], ident[:, :])
                t.then_inc(late_turned, 1)

            pe.sem_inc(turned, rows_free + SKIPPED)
            pe.wait_ge(ident_done, 1)
            for o in range(NS):
                if o < NG:
                    turn_rows(0, 0, o, first=True)
                pe.wait_ge(high_done, o + 1)
                pe.wait_ge(low_done, o + 1)
                pick(0, o)

            def pair(i, before_last=False):
                gram_blocks(i, 0, 0)
                gram_blocks(i, 0, 1)
                turn_rows(i, 1, 0)
                turn_pairs(i - 1, 1)
                gram_blocks(i, 0, 2)
                layer1_in_turn(i - 1, 0)
                gram_blocks(i, 0, 3)
                turn_rows(i, 1, 1)
                layer1_in_turn(i - 1, 1)
                turn_rows(i, 1, 2)
                pick(i + 1, 0)
                layer1_in_turn(i - 1, 2)
                turn_rows(i, 1, 3)
                pick(i + 1, 1)
                turn_rows(i, 1, 4)
                turn_rows(i, 1, 5)
                layer1_in_turn(i - 1, 3)

                gram_blocks(i, 1, 0)
                pick(i + 1, 2)
                turn_rows(i + 1, 0, 0)
                gram_blocks(i, 1, 1)
                turn_pairs(i, 0)
                pick(i + 1, 3)
                turn_rows(i + 1, 0, 1)
                gram_blocks(i, 1, 2)
                pick(i + 1, 4)
                layer2_in_turn(i - 1, 0)
                turn_rows(i + 1, 0, 2)
                gram_blocks(i, 1, 3)
                if not before_last:
                    pick(i + 1, 5)
                turn_rows(i + 1, 0, 3)
                if before_last:
                    turn_late(0)
                turn_rows(i + 1, 0, 4)
                if not before_last:
                    pick(i + 1, 6)
                turn_rows(i + 1, 0, 5)
                layer2_in_turn(i - 1, 1)

            turn_rows(0, 1, 0, first=True)
            gram_blocks(0, 0, 0)
            gram_blocks(0, 0, 1)
            turn_rows(0, 1, 1, first=True)
            pick(1, 0)
            gram_blocks(0, 0, 2)
            turn_rows(0, 1, 2, first=True)
            pick(1, 1)
            gram_blocks(0, 0, 3)
            pick(1, 2)
            turn_rows(0, 1, 3, first=True)
            pick(1, 3)
            turn_rows(0, 1, 4, first=True)
            turn_rows(0, 1, 5, first=True)

            pick(1, 4)
            gram_blocks(0, 1, 0)
            turn_rows(1, 0, 0)
            gram_blocks(0, 1, 1)
            pick(1, 5)
            turn_pairs(0, 0)
            turn_rows(1, 0, 1)
            gram_blocks(0, 1, 2)
            turn_rows(1, 0, 2)
            turn_rows(1, 0, 3)
            pick(1, 6)
            turn_rows(1, 0, 4)
            turn_rows(1, 0, 5)
            gram_blocks(0, 1, 3)

            pe.wait_ge(w1z_in, 16 * ZC)
            pe.wait_ge(w1d_done, 1)
            pe.wait_ge(mlp_in, 80)
            with pe.Fori(1, NP - 2) as i:
                pair(i)
            pair(NP - 2, before_last=True)

            i = NP - 1
            gram_blocks(i, 0, 0, last=True)
            gram_blocks(i, 0, 1)
            gram_blocks(i, 0, 2)
            turn_rows(i, 1, 0)
            turn_pairs(i - 1, 1)
            turn_late(1)
            gram_blocks(i, 0, 3)
            pe.wait_ge(second_taken, (i - 1) * 2 + 1)
            layer1(i - 1, 0)
            turn_rows(i, 1, 1)
            pe.wait_ge(late_taken, 2)
            layer1(i - 1, 1, ps=pick_ps)
            pe.wait_ge(hidden_taken, (i - 1) * C1 + 1)
            layer1(i - 1, 2)
            turn_rows(i, 1, 2)
            pe.wait_ge(hidden_taken, (i - 1) * C1 + 2)
            layer1(i - 1, 3, ps=pick_ps)
            pe.wait_ge(hidden_taken, (i - 1) * C1 + 3)
            layer2(i - 1, 0, taken=(i - 1) * C1 + C1)
            turn_rows(i, 1, 3)
            turn_rows(i, 1, 4)
            layer2(i - 1, 1, ps=pick_ps)
            turn_rows(i, 1, 5)
            turn_pairs(i, 0, last=True)
            gram_blocks(i, 1, 0, last=True)
            gram_blocks(i, 1, 1)
            gram_blocks(i, 1, 2)
            gram_blocks(i, 1, 3)
            pe.wait_ge(second_taken, i * 2)
            layer1(i, 0, half=0, last=True)
            pe.wait_ge(second_taken, i * 2 + 1)
            layer1(i, 1, ps=pick_ps, half=0)
            pe.wait_ge(hidden_taken, i * C1 + 1)
            layer1(i, 2, half=0)
            pe.wait_ge(hidden_taken, i * C1 + 2)
            layer1(i, 3, ps=pick_ps, half=0)
            turn_pairs(i, 1, last=True)
            pe.wait_ge(hidden_taken, i * C1 + 3)
            layer2(i, 0, taken=i * C1 + C1)
            layer1(i, 0, ps=pick_ps, half=1, last=True)
            pe.wait_ge(second_taken, i * 2 + 2)
            layer1(i, 1, half=1)
            pe.wait_ge(hidden_taken, (i + 1) * C1 + 1)
            layer1(i, 2, ps=pick_ps, half=1)
            pe.wait_ge(hidden_taken, (i + 1) * C1 + 2)
            layer1(i, 3, half=1)
            pe.wait_ge(hidden_taken, (i + 1) * C1 + 3)
            layer2(i, 1, ps=pick_ps, taken=(i + 1) * C1 + C1)
            pe.wait_ge(scored, NP * 2)
            pe.transpose(mlp_ps[0:B // P, 0:P], y[:, :], ident[:, :]).then_inc(y_turned, 1)

        @block.vector
        def _(dve):
            def convert_ids(i):
                dve.wait_ge(ids_b_in, i * 16 + 16)
                dve.tensor_scalar(ids_s[:, :, :], ids_b[:, :, :], row_id[:, 0:1], None, ALU.subtract)\
                    .then_inc(ids_s_done, 1)

            def make_onehot(i, o, first=False):
                dve.wait_ge(ids_s_done, i + 1)
                if o >= RING:
                    dve.wait_ge(picked, i * NS + (o - RING + 1))
                elif not first:
                    before = max(k for k in range(NS) if k % RING == o)
                    dve.wait_ge(picked, i * NS - (NS - before - 1))
                for c in range(CHUNKS):
                    t = dve.tensor_scalar(onehot[:, o % RING, c, :], ids_s[:, o, :], float(c),
                                          None, ALU.is_equal)
                t.then_inc(onehot_done, 1)

            def cut_leading(o, table, to):
                dve.wait_ge(table_in[o], 16)
                dve.tensor_scalar(to.bitcast(U32), table.bitcast(U32), LEADING, None, ALU.bitwise_and)\
                    .then_inc(leading_done, 1)

            def make_low(o, table, cut):
                dve.wait_ge(leading_done, o + 1)
                dve.tensor_tensor(parts[:, o, 1, :], table, cut, ALU.subtract).then_inc(low_done, 1)

            def place_late(u):
                dve.wait_ge(late_turned, u + 1)
                dve.tensor_copy(feat[:, u, :, S0 - NL:S0].rearrange("d p s -> d s p"),
                                pick_bank[:, 0:NL * P].rearrange("d (s p) -> d s p", p=P)).then_inc(late_taken, 1)

            def place_staged(i, u, last=False):
                slots = S0 - NL if last else S0
                dve.wait_ge(pick_taken, i * NS + (slots))
                dve.wait_ge(staged_in, i * 16 + 16)
                dve.tensor_copy(feat[:, u, :, 0:slots].rearrange("d p s -> d s p"),
                                staged[:, 0:slots, u * P:(u + 1) * P]).then_inc(staged_taken, 1)

            def place_rows(i, u, g, first=False):
                a, b = GROUPS[g]
                dve.wait_ge(turned, group_turn(i, u, g) + (rows_free + 1))
                dve.tensor_copy(feat[:, u, :, a:b].rearrange("d p s -> d s p"),
                                turn_ps[:, turn_bank(u, g, first), 0:(b - a) * P]
                                .rearrange("d (s p) -> d s p", p=P)).then_inc(turn_taken, 1)

            def make_z(i, u):
                dve.wait_ge(gram_taken, i * (2 * GRAMS) + ((u + 1) * GRAMS + 2))
                dve.transpose(z[:, u, 0:F, :], gram[:, u, :, :])
                dve.transpose(z[:, u, F:F + K_MAX, :], gram[:, u, 0:K_MAX, :]).then_inc(z_done, 1)
                dve.wait_ge(z_done, i * 2 + (u + 3))
                flat = z[:, u, :, :].rearrange("p g f -> p (g f)")
                diagonals = bass.AP(flat.tensor, flat.offset + SUB,
                                    [list(flat.ap[0]), [SUB, K_MAX], [SUB + 1, F]])
                dve.tensor_copy(pairs[:, u, :, :], diagonals).then_inc(pairs_done, 1)

            def place_pairs(i, u, last=False):
                dve.wait_ge(turned, pairs_turn(i, u, last) + (rows_free + 1))
                dve.tensor_copy(zt[0:ZK, 0:ZC, u * P:(u + 1) * P].rearrange("k c (j s) -> k c s j", s=QUADS),
                                turn_ps[0:ZK, pairs_bank(u, last), 0:ZC * P]
                                .rearrange("k (c s j) -> k c s j", c=ZC, s=QUADS))\
                    .then_inc(turn_taken, 1)

            dve.sem_inc(turn_taken, BANKS + SKIPPED)
            dve.memset(feat[:, 0, :, F:SUB], 0.0).then_inc(feat_zero, 1)
            for u in range(2):
                dve.memset(gram[:, u, :, :], 0.0).then_inc(z_done, 1)
            dve.wait_ge(row_i_done, 1)
            dve.tensor_copy(row_id[:, :], row_i[:, :]).then_inc(row_id_done, 1)
            dve.wait_ge(row_id_done, 1)
            for o in range(NS):
                if o >= 2:
                    dve.wait_ge(high_done, o - 1)
                cut_leading(o, tables_s[o % STAGES], leading[o % 2])
                if o == 0:
                    make_low(o, tables_s[o % STAGES], leading[o % 2])
                    convert_ids(0)
                make_onehot(0, o, first=True)
                if o > 0:
                    make_low(o, tables_s[o % STAGES], leading[o % 2])
            dve.wait_ge(onehot_done, NS)
            convert_ids(1)
            place_staged(0, 0)
            dve.memset(feat[:, 1, :, F:SUB], 0.0).then_inc(feat_zero, 1)

            def score(i, u, ps=mlp_ps):
                dve.wait_ge(second, i * 2 + (u + 1))
                dve.tensor_tensor(h2[:, u, :], ps, b2s[:, :], ALU.add).then_inc(second_taken, 1)
                dve.wait_ge(second_taken, i * 2 + (u + 2))
                dve.scalar_tensor_tensor(h2w[:, u, :], h2[:, u, :], 0.0, w3s[:, :], ALU.max, ALU.mult,
                                         accum_out=y[:, bass.ds(i * 2 + u, 1)]).then_inc(scored, 1)

            def pair(i, before_last=False):
                place_rows(i, 1, 0)
                place_pairs(i - 1, 1)
                place_staged(i, 1)
                convert_ids(i + 1)
                make_onehot(i + 1, 0)
                place_rows(i, 1, 1)
                make_z(i, 0)
                place_rows(i, 1, 2)
                make_onehot(i + 1, 1)
                make_onehot(i + 1, 2)
                place_rows(i, 1, 3)
                place_rows(i, 1, 4)
                place_rows(i, 1, 5)
                make_onehot(i + 1, 3)

                place_rows(i + 1, 0, 0)
                make_onehot(i + 1, 4)
                place_pairs(i, 0)
                place_rows(i + 1, 0, 1)
                if not before_last:
                    make_onehot(i + 1, 5)
                place_rows(i + 1, 0, 2)
                score(i - 1, 0)
                if not before_last:
                    make_onehot(i + 1, 6)
                place_rows(i + 1, 0, 3)
                if before_last:
                    place_late(0)
                place_rows(i + 1, 0, 4)
                place_rows(i + 1, 0, 5)
                place_staged(i + 1, 0, last=before_last)
                make_z(i, 1)
                score(i - 1, 1)

            dve.sem_inc(second_taken, 1)
            place_staged(0, 1)
            place_rows(0, 1, 0, first=True)
            make_onehot(1, 0)
            place_rows(0, 1, 1, first=True)
            make_onehot(1, 1)
            make_onehot(1, 2)
            place_rows(0, 1, 2, first=True)
            make_onehot(1, 3)
            make_onehot(1, 4)
            place_rows(0, 1, 3, first=True)
            place_rows(0, 1, 4, first=True)
            make_onehot(1, 5)
            place_rows(0, 1, 5, first=True)

            make_z(0, 0)
            place_rows(1, 0, 0)
            make_onehot(1, 6)
            place_pairs(0, 0)
            place_rows(1, 0, 1)
            place_rows(1, 0, 2)
            dve.wait_ge(w1ab_in, 32)
            dve.tensor_tensor(w1d[:, :], w1ab[:, 0, :], w1ab[:, 1, :], ALU.add).then_inc(w1d_done, 1)
            place_rows(1, 0, 3)
            place_rows(1, 0, 4)
            place_rows(1, 0, 5)
            place_staged(1, 0)
            make_z(0, 1)
            dve.wait_ge(mlp_in, 80)
            with dve.Fori(1, NP - 2) as i:
                pair(i)
            pair(NP - 2, before_last=True)

            i = NP - 1
            place_staged(i, 1, last=True)
            place_rows(i, 1, 0)
            place_pairs(i - 1, 1)
            place_late(1)
            make_z(i, 0)
            place_rows(i, 1, 1)
            place_rows(i, 1, 2)
            score(i - 1, 0)
            place_rows(i, 1, 3)
            place_rows(i, 1, 4)
            place_rows(i, 1, 5)
            place_pairs(i, 0, last=True)
            score(i - 1, 1, ps=pick_ps)
            make_z(i, 1)
            place_pairs(i, 1, last=True)
            score(i, 0)
            score(i, 1, ps=pick_ps)
            dve.wait_ge(y_turned, 1)
            dve.tensor_copy(yt[:, :], mlp_ps[0:B // P, 0:P]).then_inc(yt_done, 1)

        @block.scalar
        def _(act):
            def keep_grams(i, u, c):
                if c == 0:
                    act.wait_ge(z_done, i * 2 + (u + 1))
                act.wait_ge(grammed, i * (2 * GRAMS) + (u * GRAMS + c + 1))
                blocks = gram_ps[:, c % 2, :].rearrange("p (j x) -> p j x", j=GB)
                for s in range(QUADS):
                    q = slice(s * SUB, s * SUB + F)
                    t = act.activation(gram[q, u, :, c * GB:(c + 1) * GB].rearrange("p g j -> p j g"),
                                       blocks[q, :, s * F:(s + 1) * F], ACT.Copy)
                t.then_inc(gram_taken, 1)

            def place_first_rows(g):
                a, b = GROUPS[g]
                act.wait_ge(turned, group_turn(0, 0, g) + (rows_free + 1))
                act.activation(feat[:, 0, :, a:b].rearrange("d p s -> d s p"),
                               turn_ps[:, turn_bank(0, g, True), 0:(b - a) * P]
                               .rearrange("d (s p) -> d s p", p=P), ACT.Copy).then_inc(turn_taken, 1)

            def keep_pick(i, o):
                act.wait_ge(picked, i * NS + (o + 1))
                act.activation(staged[:, 1 + o, :], pick_ps, ACT.Copy).then_inc(pick_taken, 1)

            def keep_hidden(i, n, ps=mlp_ps, half=None):
                x = columns(half)
                act.wait_ge(hidden, i * C1 + (n + 1 + (C1 if half == 1 else 0)))
                act.activation(h1[:, n, x], ps[:, x], ACT.Relu, bias=b1s[:, n:n + 1]).then_inc(hidden_taken, 1)

            def make_high(o, cut):
                act.wait_ge(leading_done, o + 1)
                act.activation(parts[:, o, 0, :], cut, ACT.Copy).then_inc(high_done, 1)

            act.sem_inc(gram_taken, 2)
            act.sem_inc(pick_taken, 1)
            for o in range(NS):
                make_high(o, leading[o % 2])
                if o > 0:
                    keep_pick(0, o - 1)
                    place_first_rows(o - 1)
            keep_pick(0, NS - 1)

            def pair(i, before_last=False):
                keep_grams(i, 0, 0)
                keep_grams(i, 0, 1)
                keep_grams(i, 0, 2)
                keep_hidden(i - 1, 0)
                keep_grams(i, 0, 3)
                keep_hidden(i - 1, 1)
                act.wait_ge(staged_taken, i * 2 + 2)
                keep_pick(i + 1, 0)
                keep_hidden(i - 1, 2)
                keep_pick(i + 1, 1)
                keep_hidden(i - 1, 3)
                keep_grams(i, 1, 0)
                keep_pick(i + 1, 2)
                keep_grams(i, 1, 1)
                keep_pick(i + 1, 3)
                keep_grams(i, 1, 2)
                keep_pick(i + 1, 4)
                keep_grams(i, 1, 3)
                if not before_last:
                    keep_pick(i + 1, 5)
                    keep_pick(i + 1, 6)

            keep_grams(0, 0, 0)
            keep_grams(0, 0, 1)
            act.wait_ge(staged_taken, 2)
            keep_pick(1, 0)
            keep_grams(0, 0, 2)
            keep_pick(1, 1)
            keep_grams(0, 0, 3)
            keep_pick(1, 2)
            keep_pick(1, 3)
            keep_pick(1, 4)
            keep_grams(0, 1, 0)
            keep_grams(0, 1, 1)
            keep_pick(1, 5)
            keep_grams(0, 1, 2)
            keep_pick(1, 6)
            keep_grams(0, 1, 3)
            act.wait_ge(mlp_in, 80)
            with act.Fori(1, NP - 2) as i:
                pair(i)
            pair(NP - 2, before_last=True)

            i = NP - 1
            for c in range(GRAMS):
                keep_grams(i, 0, c)
            for n in range(C1):
                keep_hidden(i - 1, n, ps=pick_ps if n % 2 else mlp_ps)
            for c in range(GRAMS):
                keep_grams(i, 1, c)
            for half in range(2):
                for n in range(C1):
                    keep_hidden(i, n, ps=pick_ps if (n + half) % 2 else mlp_ps, half=half)


def kernel(**inputs):
    import numpy as np
    import concourse.bacc as bacc
    from concourse.bass_utils import run_bass_kernel_spmd as run

    a = {k: np.asarray(v) for k, v in inputs.items()}
    ids, w1 = a["ids"], a["W_top1"]
    arrays = {
        "dense_t": a["r_dense_output"].T,
        "ids_fetched": ids[:, FETCHED + LATE],
        "ids_selected": ids[:, SELECTED].T,
        "w1_pairs": w1[pair_rows()],
        "w1_dense": np.stack([w1[:D], w1[D + PAIRS:]]),
        "w2": a["W_top2"],
        "w3": a["W_top3"].reshape(1, -1),
        "b1": a["b_top1"].reshape(-1, P).T,
        "b2": a["b_top2"].reshape(1, -1),
    }
    arrays |= {f"tbl_{f}": a[f"tbl_{f}"] for f in range(len(TABLE_ROWS))}
    arrays = {k: np.ascontiguousarray(v) for k, v in arrays.items()}

    nc = bacc.Bacc("TRN2", target_bir_lowering=False, num_devices=1)
    ap = {k: nc.dram_tensor(k, v.shape, mybir.dt.from_np(v.dtype), kind="ExternalInput").ap()
          for k, v in arrays.items()}
    out = nc.dram_tensor("y_out_dram", (ids.shape[0], 1), F32, kind="ExternalOutput").ap()
    tower(nc, ap["dense_t"], ap["ids_fetched"], ap["ids_selected"],
          [ap[f"tbl_{f}"] for f in range(len(TABLE_ROWS))], ap["w1_pairs"], ap["w1_dense"],
          ap["w2"], ap["w3"], ap["b1"], ap["b2"], out)
    return run(nc, [arrays], core_ids=[0]).results[0]["y_out_dram"]
```
